# Optimizing a Trainium2 kernel written in Bass

```python
import numpy as np
import jax
import jax.numpy as jnp

def _softmax(x, axis=-1):
    return jax.nn.softmax(x, axis=axis)

def _gelu(x):
    return jax.nn.gelu(x, approximate=True)

def _silu(x):
    return jax.nn.silu(x)

def _sigmoid(x):
    return jax.nn.sigmoid(x)

def _layernorm(x, axis=-1, eps=1e-05):
    m = jnp.mean(x, axis=axis, keepdims=True)
    v = jnp.var(x, axis=axis, keepdims=True)
    return (x - m) / jnp.sqrt(v + eps)

def _scatter_add(tgt, idx, src, axis=0):
    return tgt.at[idx].add(src)

def _segment_sum(src, seg, n):
    return jax.ops.segment_sum(src, seg, n)
kernel_name = 'mk_gnn_preln_d1_gnn_r8_9416da'

def setup_inputs(seed: int=0):
    np.random.seed(seed)
    _w = jnp.asarray

    def _rec_inputs():
        import jax
        import jax.numpy as jnp
        _gk = jax.random.key(seed)
        x = -0.0001978 + 0.9998 * jax.random.normal(jax.random.fold_in(_gk, 1), (6250, 128), jnp.float32)
        src = jax.random.randint(jax.random.fold_in(_gk, 2), (100000,), 0, 6250, jnp.int32)
        dst = jax.random.randint(jax.random.fold_in(_gk, 3), (100000,), 0, 6250, jnp.int32)
        _o = jnp.argsort(dst, stable=True)
        src = src[_o]
        dst = dst[_o]
        return (x, src, dst)
    x, src, dst = _rec_inputs()

    def _L0_gnn_setup():
        import jax, jax.numpy as jnp
        import numpy as np
        N_NODES = 6250
        N_EDGES = 100000
        D_MODEL = 128
        N_HEAD = 8
        key = jax.random.key(seed)
        k_e, k_x, k_q, k_k, k_v = jax.random.split(key, 5)
        bound = float(np.sqrt(6.0 / (D_MODEL + D_MODEL)))
        return {'edge_index': jax.random.randint(k_e, (2, N_EDGES), 0, N_NODES, dtype=jnp.int64), 'embeds': jax.random.normal(k_x, (N_NODES, D_MODEL), dtype=jnp.float32), 'Wq': jax.random.uniform(k_q, (D_MODEL, D_MODEL), jnp.float32, -bound, bound), 'Wk': jax.random.uniform(k_k, (D_MODEL, D_MODEL), jnp.float32, -bound, bound), 'Wv': jax.random.uniform(k_v, (D_MODEL, D_MODEL), jnp.float32, -bound, bound), 'gamma': jnp.ones((D_MODEL,), jnp.float32), 'beta': jnp.zeros((D_MODEL,), jnp.float32), 'n_head': N_HEAD}
    _L0_gnn_all = _L0_gnn_setup()
    _L0_gnn_in = {k: v for k, v in _L0_gnn_all.items() if k in ('Wq', 'Wk', 'Wv', 'gamma', 'beta')}
    del _L0_gnn_all
    return {'x': x, 'src': src, 'dst': dst, 'L0_gnn_Wq': _L0_gnn_in['Wq'], 'L0_gnn_Wk': _L0_gnn_in['Wk'], 'L0_gnn_Wv': _L0_gnn_in['Wv'], 'L0_gnn_gamma': _L0_gnn_in['gamma'], 'L0_gnn_beta': _L0_gnn_in['beta']}

def reference(x, src, dst, L0_gnn_Wq, L0_gnn_Wk, L0_gnn_Wv, L0_gnn_gamma, L0_gnn_beta):
    import jax
    import jax.numpy as jnp

    def _L0_gnn_ref(edge_index, embeds, Wq, Wk, Wv, gamma, beta, n_head):
        import jax, jax.numpy as jnp
        import numpy as np
        N_NODES = 6250
        N_EDGES = 100000
        D_MODEL = 128
        N_HEAD = 8
        rows, cols = (edge_index[0], edge_index[1])
        nvar, d_model = embeds.shape
        evar = rows.shape[0]
        hd = d_model // n_head
        rowE = embeds[rows]
        colE = embeds[cols]
        qE = (rowE @ Wq).reshape(evar, n_head, hd)
        kE = (colE @ Wk).reshape(evar, n_head, hd)
        vE = (colE @ Wv).reshape(evar, n_head, hd)
        att = jnp.einsum('ehd,ehd->eh', qE, kE)
        att = jnp.clip(att, -10.0, 10.0)
        expAtt = jnp.exp(att)
        attNorm = jax.ops.segment_sum(expAtt, rows, num_segments=nvar)[rows]
        att = expAtt / (attNorm + 1e-08)
        resE = (att[..., None] * vE).reshape(evar, d_model)
        res = jax.ops.segment_sum(resE, rows, num_segments=nvar)
        res = res + embeds
        mean = jnp.mean(res, axis=-1, keepdims=True)
        var = jnp.mean(jnp.square(res - mean), axis=-1, keepdims=True)
        res = (res - mean) * jax.lax.rsqrt(var + 1e-06) * gamma + beta
        return res
    edge_index = jnp.stack([src, dst])
    h = jnp.maximum(_layernorm(x, axis=-1), 0.0)
    x = x + _L0_gnn_ref(edge_index, h, L0_gnn_Wq, L0_gnn_Wk, L0_gnn_Wv, L0_gnn_gamma, L0_gnn_beta, 8)
    return x

_drawn_inputs = setup_inputs


def setup_inputs(seed=0):
    import zlib

    import numpy as np

    out = dict(_drawn_inputs(seed))
    spreads = {'L0_gnn_gamma': (1.0, 0.2), 'L0_gnn_beta': (0.0, 0.1)}
    factors = {}
    for name, (base, spread) in spreads.items():
        noise = np.random.default_rng([zlib.crc32(name.encode()), seed]).standard_normal(out[name].shape)
        drawn = base * np.exp(spread * noise) if base else spread * noise
        out[name] = jnp.asarray(drawn.astype(out[name].dtype))
    for name, factor in factors.items():
        out[name] = (out[name] * factor).astype(out[name].dtype)
    return out
```

```python
from contextlib import ExitStack

import numpy as np

import concourse.bass as bass
from concourse import mybir

F32 = mybir.dt.float32
BF16 = mybir.dt.bfloat16
I32 = mybir.dt.int32
U32 = mybir.dt.uint32
ALU = mybir.AluOpType
ACT = mybir.ActivationFunctionType
AX = mybir.AxisListType

P = 128
N_NODES = 6250
N_EDGES = 100000
D = 128
N_HEAD = 8
HD = D // N_HEAD
NB = -(-N_NODES // P)
TAIL = N_NODES - (NB - 1) * P

CB = 7
CP = 112
NT = CB * CP
TW = CB * P
SHIFT = 13
FIELD = (1 << SHIFT) - 1
FLOAT_BIT = 0x40000000
LOW = 7
HIGH = (NT - 1).bit_length()
REAL_TILES = -(-N_EDGES // P)
assert N_NODES < FIELD and REAL_TILES <= NT and (1 << LOW) == P

G = 4
U = 4
GROUPS = -(-(REAL_TILES + NB - 1) // (G * U)) * U
AHEAD = 3
NV = (GROUPS + AHEAD + 1) * G
HALF = NV // 2
RW = D + N_HEAD
assert GROUPS % U == 0 and NV % 2 == 0 and HALF <= 512 and NV - (NB - 1) <= NT + P

C_IDENT = 0
C_IOTA = C_IDENT + P
C_SIGN = C_IOTA + NV
C_TILE = C_SIGN + (HIGH + 1) * CB
C_EDGE = C_TILE + CB
C_BLOCK = C_EDGE + NB - 1
C_ALL = C_BLOCK + 1


def run_signs():
    c = np.arange(NT)
    out = np.ones((HIGH + 1, NT), np.float32)
    for j in range(HIGH + 1):
        r = c >> j
        out[j][(r % 2 == 0) & (((r + 1) << j) < NT)] = -1.0
    return out


def shape_constants():
    k = np.zeros((P, C_ALL), np.float32)
    k[:, C_IDENT:C_IDENT + P] = np.eye(P)
    k[:, C_IOTA:C_IOTA + NV] = np.arange(NV)
    sign = run_signs()
    change = np.concatenate([sign[:1], sign[:-1] * sign[1:]])
    k[:CP, C_SIGN:C_TILE] = change.reshape(HIGH + 1, CB, CP).transpose(2, 0, 1).reshape(CP, -1)
    k[:CP, C_TILE:C_EDGE] = np.arange(NT).reshape(CB, CP).T
    k[:, C_EDGE:C_BLOCK] = P * np.arange(1, NB)
    k[:, C_BLOCK] = np.arange(1, P + 1)
    return k


def gnn_kernel(nc, x, src, dst, Wq, Wk, Wv, gamma, beta, consts, out):
    kv_table = nc.dram_tensor("kv_table", [NB * P, 2 * D], F32, kind="Internal").ap()
    with ExitStack() as ctx:
        def sb(name, shape, dt=F32):
            return ctx.enter_context(nc.sbuf_tensor(name, shape, dt))

        def sem(name):
            return ctx.enter_context(nc.semaphore(name))

        const = sb("const", [P, C_ALL])
        X = sb("X", [P, NB, D])
        H = sb("H", [P, NB, D])
        acc = sb("acc", [P, NB, RW])
        qf = acc[:].rearrange("p b w -> p (b w)")[:, 0:NB * D]
        qs = sb("qs", [P, 3, NB * D], BF16)
        kv = sb("kv", [P, U, G, 2 * D])
        STG = 7
        stage = kv[:].rearrange("p u g w -> p (u g w)").rearrange("p (r w) -> p r w", r=2)[
            :, :, 0:STG * 2 * D].rearrange("p r (b w) -> p r b w", b=STG)
        key = [sb("key0", [P, TW]), sb("key1", [P, TW])]
        part = sb("part", [P, 4, TW], BF16)
        part_i = kv[:].rearrange("p u g w -> p (u g w)").bitcast(I32)[:, 0:4 * TW].rearrange(
            "p (k w) -> p k w", k=4)
        tile_of = sb("tile_of", [P, NV])
        lsrc = sb("lsrc", [P, NV])
        dstf = sb("dstf", [P, NV])
        blk_i = sb("blk_i", [1, NV], I32)
        pick = sb("pick", [P, CB, NV], BF16)
        below = sb("below", [P, CB, NB - 1], BF16)
        passed = sb("passed", [P, NV], BF16)
        start = sb("start", [P, 1])
        last_src = sb("last_src", [P, CB])
        ones = sb("ones", [P, P], BF16)
        W = sb("W", [P, 3 * D])
        gam = sb("gam", [P, D])
        bet = sb("bet", [P, D])
        hT = sb("hT", [P, 2, D])
        stat = sb("stat", [P, 6, NB])
        eps = sb("eps", [P, 2])
        idx = sb("idx", [P, U, G], U32)
        S = sb("S", [P, U, G, P])
        ST = sb("ST", [P, 2, G, P], BF16)
        prod = sb("prod", [P, G * D])
        upper = prod
        att = sb("att", [P, G * N_HEAD])
        attc = sb("attc", [P, 2, G * N_HEAD])
        wv = sb("wv", [P, 2, G, RW])
        rden = sb("rden", [P, NB, N_HEAD])
        bn = sb("bn", [P, NB, 6])
        mv = sb("mv", [P, NB, 2])
        fin = sb("fin", [P, 3, NB])

        ident = const[:, C_IDENT:C_IDENT + P]
        iota = const[:, C_IOTA:C_IOTA + NV]

        psum = ctx.enter_context(nc.psum_tensor("psum", [P, 8, 512], F32))
        flat = psum[:].rearrange("p b w -> p (b w)")
        slots_ps = flat[:, 0:NT]
        tiles_ps = flat[:, 1024:1024 + TW]
        hT_ps = lambda b: psum[:, 4 + b % 2, 0:D]
        qkv_ps = lambda b: psum[:, 6 + b % 2, 0:3 * D]
        start_ps = psum[0:NB - 1, 2, 0:1]
        blk_ps = psum[:, 4:6, 0:HALF]
        vsrc_ps = psum[:, 6:8, 0:HALF]
        vdst_ps = psum[:, 0:2, 0:HALF]
        q_ps = lambda i: psum[:, i % 2, :]
        st_ps = lambda i: psum[:, 2 + i % 2, :]
        sum_ps = lambda i, v: psum[:, 4 + 2 * (i % 2) + v // 2, (v % 2) * RW:(v % 2 + 1) * RW]
        w_ps = lambda i: psum[:, i % 2, 0:G * N_HEAD]

        const_in = sem("const_in")
        src_in = sem("src_in")
        dst_in = sem("dst_in")
        x_in = sem("x_in")
        x_tail_in = sem("x_tail_in")
        w_in = sem("w_in")
        affine_in = sem("affine_in")
        pads_set = sem("pads_set")
        pool_set = sem("pool_set")
        cmp_done = sem("cmp_done")
        turned = sem("turned")
        sums_done = sem("sums_done")
        negmean_done = sem("negmean_done")
        squares_done = sem("squares_done")
        std_done = sem("std_done")
        rstd_done = sem("rstd_done")
        nmr_done = sem("nmr_done")
        h_done = sem("h_done")
        hT_ps_done = sem("hT_ps_done")
        hT_done = sem("hT_done")
        qkv_done = sem("qkv_done")
        kv_staged = sem("kv_staged")
        qf_done = sem("qf_done")
        kv_stored = [sem("kv_stored0"), sem("kv_stored1")]
        split_done = sem("split_done")
        xb_done = sem("xb_done")
        acc_zeroed = sem("acc_zeroed")
        fields_done = sem("fields_done")
        parts_done = sem("parts_done")
        below_done = sem("below_done")
        start_summed = sem("start_summed")
        set_up = sem("set_up")
        blocks_summed = sem("blocks_summed")
        visits_picked = sem("visits_picked")
        dstf_done = sem("dstf_done")
        blk_done = sem("blk_done")
        idx_ready = sem("idx_ready")
        gathers_begun = sem("gathers_begun")
        kv_landed = [sem(f"kv_landed{u}") for u in range(U)]
        s_made = sem("s_made")
        st_turned = sem("st_turned")
        st_copied = sem("st_copied")
        q_spread = sem("q_spread")
        prod_done = sem("prod_done")
        red_done = sem("red_done")
        clip_done = sem("clip_done")
        exp_done = sem("exp_done")
        expw_done = sem("expw_done")
        wv_done = sem("wv_done")
        summed = sem("summed")
        added = sem("added")
        fin_v = sem("fin_v")
        fin_std = sem("fin_std")
        fin_norm = sem("fin_norm")
        fin_gam = sem("fin_gam")
        fin_out = sem("fin_out")
        stored = sem("stored")

        CHUNKS = [range(a, min(a + STG, NB)) for a in range(0, NB, STG)]

        FV_STATS, FV_NMR, steps = [], [], 2
        for n in range(len(CHUNKS) + 1):
            if n < len(CHUNKS):
                steps += 2 + 2 * len(CHUNKS[n])
                FV_STATS.append(steps)
            if n >= 1:
                steps += 2
                FV_NMR.append(steps)

        def after(eng, semaphore, value):
            if not isinstance(value, int) or value > 0:
                eng.wait_ge(semaphore, value)

        def pieces(d):
            full, rem = NT // (2 * d), NT % (2 * d)
            base = 2 * d * full
            pairs = [(0, full, d)] if full else []
            if rem > d:
                pairs.append((base, 1, rem - d))
                lone = (base + rem - d, 2 * d - rem)
            else:
                lone = (base, rem)
            return pairs, lone

        count = [3]

        def counted(n):
            count[0] += n
            return count[0]

        after_sign = [counted(1)]
        after_high, after_low = [0], [counted(LOW * (LOW + 1))]
        buf_sign, buf_high = [1], [0]
        buf = (1 + LOW * (LOW + 1) // 2) % 2
        for j in range(1, HIGH + 1):
            after_sign.append(counted(1))
            buf_sign.append(buf ^ 1)
            for d in (1 << e for e in reversed(range(j))):
                pairs, lone = pieces(d)
                counted((3 if d == 1 << (j - 1) else 2) * len(pairs) + (1 if lone[1] else 0))
            after_high.append(count[0])
            buf_high.append((buf + 1 + j) % 2)
            after_low.append(counted(2 * LOW + 1))
            buf = (buf + 1 + j + LOW) % 2

        block = ctx.enter_context(nc.Block())

        @block.sync
        def _(sp):
            whole = (CB - 1) * CP * P
            rest = (N_EDGES - whole) // P
            odd = N_EDGES - whole - rest * P
            sp.dma_start(const[:], consts).then_inc(const_in, 16)
            for edges, raw, landed in ((src, key[0], src_in), (dst, key[1], dst_in)):
                r = raw[:].bitcast(I32)
                if edges is src:
                    sp.wait_ge(pads_set, 2)
                sp.dma_start(r[0:CP, 0:(CB - 1) * P].rearrange("p (b m) -> p b m", b=CB - 1),
                             edges[0:whole].rearrange("(b p m) -> p b m", b=CB - 1, p=CP)
                             ).then_inc(landed, 16)
                sp.dma_start(r[0:rest, (CB - 1) * P:TW],
                             edges[whole:whole + rest * P].rearrange("(p m) -> p m", p=rest)
                             ).then_inc(landed, 16)
                sp.dma_start(r[rest:rest + 1, (CB - 1) * P:(CB - 1) * P + odd],
                             edges[whole + rest * P:N_EDGES].rearrange("(a m) -> a m", a=1)
                             ).then_inc(landed, 16)
            sp.dma_start(X[:, 0:NB - 1, :], x[0:(NB - 1) * P, :].rearrange("(b p) d -> p b d", p=P)
                         ).then_inc(x_in, 16)
            sp.wait_ge(pool_set, 1)
            sp.dma_start(X[0:TAIL, NB - 1, :], x[(NB - 1) * P:N_NODES, :]).then_inc(x_tail_in, 16)
            for n, w in enumerate((Wk, Wv, Wq)):
                sp.dma_start(W[:, n * D:(n + 1) * D], w).then_inc(w_in, 16)
            for row, a in ((gam, gamma), (bet, beta)):
                sp.dma_start(row[:], a.rearrange("(o d) -> o d", o=1).to_broadcast([P, D])
                             ).then_inc(affine_in, 16)
            for n, blocks in enumerate(CHUNKS):
                sp.wait_ge(kv_staged, blocks[-1] + 1)
                sp.dma_start(
                    kv_table[blocks[0] * P:(blocks[-1] + 1) * P, :].rearrange("(b p) w -> p b w", p=P),
                    stage[:, n % 2, 0:len(blocks), :]).then_inc(kv_stored[n % 2], 16)
            for n, blocks in enumerate(CHUNKS):
                sp.wait_ge(fin_out, n + 1)
                whole_blocks = [b for b in blocks if b < NB - 1]
                a, e = whole_blocks[0], whole_blocks[-1] + 1
                sp.dma_start(out[a * P:e * P, :].rearrange("(b p) d -> p b d", p=P),
                             X[:, a:e, :]).then_inc(stored, 16)
                if len(whole_blocks) < len(blocks):
                    sp.dma_start(out[(NB - 1) * P:N_NODES, :], X[0:TAIL, NB - 1, :]
                                 ).then_inc(stored, 16)
            sp.wait_ge(stored, 16 * (len(CHUNKS) + 1))

        @block.gpsimd
        def _(pool):
            pool.memset(X[:, NB - 1, :], 0.0).then_inc(pool_set, 1)
            pool.memset(eps[:, 0:1], 1e-5).then_inc(pool_set, 1)
            pool.memset(eps[:, 1:2], 1e-6).then_inc(pool_set, 1)
            pool.memset(ones[:], 1.0).then_inc(pool_set, 1)
            pool.wait_ge(sums_done, NB)
            pool.tensor_scalar(stat[:, 1, :], stat[:, 0, :], -1.0 / D, None, ALU.mult
                               ).then_inc(negmean_done, 1)
            pool.wait_ge(negmean_done, 1)
            pool.wait_ge(rstd_done, 1)
            pool.tensor_tensor(stat[:, 5, :], stat[:, 1, :], stat[:, 4, :], ALU.mult
                               ).then_inc(nmr_done, 1)
            for n, blocks in enumerate(CHUNKS):
                a, e = blocks[0] * D, (blocks[-1] + 1) * D
                pool.wait_ge(qf_done, blocks[-1] + 1)
                pool.tensor_copy(qs[:, 0, a:e], qf[:, a:e]).then_inc(split_done, 1)
                pool.wait_ge(split_done, 4 * n + 1)
                pool.tensor_tensor(qf[:, a:e], qf[:, a:e], qs[:, 0, a:e], ALU.subtract
                                   ).then_inc(split_done, 1)
                pool.wait_ge(split_done, 4 * n + 2)
                pool.tensor_copy(qs[:, 1, a:e], qf[:, a:e]).then_inc(split_done, 1)
                pool.wait_ge(split_done, 4 * n + 3)
                pool.tensor_tensor(qs[:, 2, a:e], qf[:, a:e], qs[:, 1, a:e], ALU.subtract
                                   ).then_inc(split_done, 1)
            pool.wait_ge(split_done, 4 * len(CHUNKS))
            pool.memset(acc[:], 0.0).then_inc(acc_zeroed, 1)
            pool.wait_ge(h_done, NB)
            pool.wait_ge(affine_in, 32)
            pool.tensor_tensor(X[:], X[:], bet[:].unsqueeze(1).to_broadcast([P, NB, D]), ALU.add
                               ).then_inc(xb_done, 1)
            for n in range(2):
                pool.wait_ge(kv_stored[n], 16 * len(CHUNKS[n::2]))

            def gathers(it):
                for u in range(U):
                    i = it * U + u
                    pool.wait_ge(idx_ready, i + 1)
                    after(pool, wv_done, i - U + 1)
                    pool.sem_inc(gathers_begun, 1)
                    for v in range(G):
                        pool.indirect_dma_start(
                            kv[:, u, v, :], None, kv_table,
                            bass.IndirectOffsetOnAxis(ap=idx[:, u, v:v + 1], axis=0)
                        ).then_inc(kv_landed[u], 16)

            gathers(0)
            with pool.Fori(1, GROUPS // U) as it:
                gathers(it)

            pool.wait_ge(affine_in, 32)
            for n, blocks in enumerate(CHUNKS):
                a, e = blocks[0], blocks[-1] + 1
                pool.wait_ge(fin_norm, e)
                pool.tensor_tensor(acc[:, a:e, 0:D], acc[:, a:e, 0:D],
                                   gam[:].unsqueeze(1).to_broadcast([P, e - a, D]), ALU.mult
                                   ).then_inc(fin_gam, 1)

        @block.tensor
        def _(pe):
            def to_slots(buf):
                for b in range(CB):
                    cut = 512 - b * CP
                    for p0, p1 in ((0, cut), (cut, CP)) if 0 < cut < CP else ((0, CP),):
                        mm = pe.transpose(slots_ps[:, b * CP + p0:b * CP + p1],
                                          buf[p0:p1, b * P:(b + 1) * P], ident[p0:p1, p0:p1])
                mm.then_inc(turned, 1)

            def to_tiles(buf):
                for b in range(CB):
                    mm = pe.transpose(tiles_ps[0:CP, b * P:(b + 1) * P],
                                      buf[:, b * CP:(b + 1) * CP], ident)
                mm.then_inc(turned, 1)

            def turn_h(b):
                pe.wait_ge(h_done, b + 1)
                if b >= 2:
                    pe.wait_ge(hT_done, b - 1)
                pe.transpose(hT_ps(b), H[:, b, :], ident).then_inc(hT_ps_done, 1)

            def project(b):
                pe.wait_ge(hT_done, b + 1)
                if b == 0:
                    pe.wait_ge(w_in, 48)
                if b >= 2:
                    pe.wait_ge(kv_staged, b - 1)
                    pe.wait_ge(qf_done, b - 1)
                pe.matmul(qkv_ps(b), hT[:, b % 2, :], W[:], start=True, stop=True
                          ).then_inc(qkv_done, 1)

            pe.wait_ge(const_in, 16)
            lot = -(-NB // (HIGH - 1))
            for j in range(1, HIGH + 1):
                pe.wait_ge(cmp_done, after_sign[j])
                to_slots(key[buf_sign[j]])
                pe.wait_ge(cmp_done, after_high[j])
                to_tiles(key[buf_high[j]])
                if j >= 2:
                    blocks = range((j - 2) * lot, min((j - 1) * lot, NB))
                    for b in blocks:
                        if b == blocks[0]:
                            turn_h(b)
                        if b + 1 in blocks:
                            turn_h(b + 1)
                        project(b)

            pe.wait_ge(below_done, 1)
            pe.wait_ge(pool_set, 4)
            for b in range(CB):
                mm = pe.matmul(start_ps, below[0:CP, b, :], ones[0:CP, 0:1],
                               start=(b == 0), stop=(b == CB - 1))
            mm.then_inc(start_summed, 1)
            pe.wait_ge(set_up, 2)
            for h in range(2):
                mm = pe.matmul(blk_ps[:, h, :], ones[0:NB - 1, :], passed[0:NB - 1, h * HALF:(h + 1) * HALF],
                               start=True, stop=True)
            mm.then_inc(blocks_summed, 1)
            pe.wait_ge(set_up, 4 + CB)
            pe.wait_ge(parts_done, 4)
            for k, into in ((2, vdst_ps), (0, vsrc_ps)):
                for h in range(2):
                    for b in range(CB):
                        for kk in (k, k + 1):
                            mm = pe.matmul(into[:, h, :], part[0:CP, kk, b * P:(b + 1) * P],
                                           pick[0:CP, b, h * HALF:(h + 1) * HALF],
                                           start=(b == 0 and kk == k), stop=(b == CB - 1 and kk == k + 1))
                mm.then_inc(visits_picked, 1)

            regs = [pe.alloc_register(f"pe_blk{v}") for v in range(G)]

            def turn(i, u):
                pe.wait_ge(s_made, i + 1)
                after(pe, st_copied, i - 1)
                for v in range(G):
                    mm = pe.transpose(st_ps(u)[:, v * P:(v + 1) * P], S[:, u % U, v, :], ident)
                mm.then_inc(st_turned, 1)

            def spread(i, u):
                pe.load(regs, blk_i[0:1, bass.ds(i * G, G)])
                pe.wait_ge(st_copied, i + 1)
                after(pe, wv_done, i - 1)
                for v in range(G):
                    at = pe.snap(regs[v], min_val=0, max_val=NB - 1)
                    for k in range(3):
                        mm = pe.matmul(q_ps(u)[:, v * D:(v + 1) * D], ST[:, u % 2, v, :],
                                       qs[:, k, bass.ds(at * D, D)], start=(k == 0), stop=(k == 2))
                mm.then_inc(q_spread, 1)

            def sums(i, u):
                pe.wait_ge(wv_done, i + 1)
                pe.wait_ge(expw_done, i + 1)
                after(pe, added, G * (i - 1))
                for v in range(G):
                    mm = pe.matmul(sum_ps(u, v), S[:, u % U, v, :], wv[:, u % 2, v, :],
                                   start=True, stop=True)
                mm.then_inc(summed, 1)

            pe.wait_ge(blk_done, 1)
            pe.wait_ge(dstf_done, 1)
            pe.wait_ge(split_done, 4 * len(CHUNKS))
            turn(0, 0)
            turn(1, 1)
            spread(0, 0)

            def body(it):
                for u in range(U):
                    i = it * U + u
                    turn(i + 2, u + 2)
                    spread(i + 1, u + 1)
                    sums(i, u)

            body(0)
            with pe.Fori(1, GROUPS // U) as it:
                body(it)

        @block.scalar
        def _(act):
            act.wait_ge(x_in, 16)
            act.wait_ge(x_tail_in, 16)
            for b in range(NB):
                act.activation(H[:, b, :], X[:, b, :], ACT.Identity, accum_out=stat[:, 0, b:b + 1]
                               ).then_inc(sums_done, 1)
            act.wait_ge(negmean_done, 1)
            act.wait_ge(sums_done, NB)
            for b in range(NB):
                act.activation(H[:, b, :], X[:, b, :], ACT.Square, bias=stat[:, 1, b:b + 1],
                               accum_out=stat[:, 2, b:b + 1]).then_inc(squares_done, 1)
            act.wait_ge(squares_done, NB)
            act.wait_ge(pool_set, 3)
            act.activation(stat[:, 3, :], stat[:, 2, :], ACT.Sqrt, scale=1.0 / D, bias=eps[:, 0:1]
                           ).then_inc(std_done, 1)
            act.wait_ge(nmr_done, 1)
            for b in range(NB):
                act.activation(H[:, b, :], X[:, b, :], ACT.Relu, scale=stat[:, 4, b:b + 1],
                               bias=stat[:, 5, b:b + 1]).then_inc(h_done, 1)

            def copy_hT(b):
                act.wait_ge(hT_ps_done, b + 1)
                if b >= 2:
                    act.wait_ge(qkv_done, b - 1)
                act.copy(hT[:, b % 2, :], hT_ps(b)).then_inc(hT_done, 1)

            copy_hT(0)
            lot = -(-NB // (HIGH - 1))
            for b in range(NB):
                if b + 1 < NB and (b + 1) % lot:
                    copy_hT(b + 1)
                act.wait_ge(qkv_done, b + 1)
                n = b // STG
                if n >= 2 and b % STG == 0:
                    act.wait_ge(kv_stored[n % 2], 16 * (n // 2))
                act.copy(qf[:, b * D:(b + 1) * D], qkv_ps(b)[:, 2 * D:3 * D]).then_inc(qf_done, 1)
                act.copy(stage[:, n % 2, b % STG, :], qkv_ps(b)[:, 0:2 * D]).then_inc(kv_staged, 1)
                if b + 1 < NB and (b + 1) % lot == 0:
                    copy_hT(b + 1)

            for n, k in enumerate((2, 3, 0, 1)):
                act.wait_ge(fields_done, n + 1)
                act.mul(part[0:CP, k, :], part_i[0:CP, k, :], 1.0 if k >= 2 else 2.0 ** -SHIFT
                        ).then_inc(parts_done, 1)
            act.wait_ge(blocks_summed, 1)
            act.wait_ge(set_up, 4)
            act.copy(blk_i[0:1, :].rearrange("p (h w) -> p h w", h=2), blk_ps[0:1, :, :]
                     ).then_inc(blk_done, 1)
            act.wait_ge(visits_picked, 1)
            act.copy(dstf[:].rearrange("p (h w) -> p h w", h=2), vdst_ps).then_inc(dstf_done, 1)
            act.wait_ge(dstf_done, 1)

            def copy_st(i, u):
                act.wait_ge(st_turned, i + 1)
                after(act, q_spread, i - 1)
                act.copy(ST[:, u % 2, :, :].rearrange("p g n -> p (g n)"), st_ps(u)
                         ).then_inc(st_copied, 1)

            def exps(i, u):
                act.wait_ge(clip_done, i + 1)
                act.activation(w_ps(u), attc[:, u % 2, :], ACT.Exp).then_inc(exp_done, 1)
                after(act, summed, i - 1)
                act.activation(wv[:, u % 2, :, D:RW],
                               attc[:, u % 2, :].rearrange("p (g h) -> p g h", g=G), ACT.Exp
                               ).then_inc(expw_done, 1)

            for i in range(AHEAD):
                act.copy(idx[:, i, :], dstf[:, i * G:(i + 1) * G]).then_inc(idx_ready, 1)
            copy_st(0, 0)
            copy_st(1, 1)

            def body(it):
                for u in range(U):
                    i = it * U + u
                    uses = it + (u + AHEAD) // U
                    after(act, kv_landed[(u + AHEAD) % U], uses * (G * 16))
                    act.copy(idx[:, (u + AHEAD) % U, :], dstf[:, bass.ds((i + AHEAD) * G, G)]
                             ).then_inc(idx_ready, 1)
                    exps(i, u)
                    copy_st(i + 2, u + 2)

            body(0)
            with act.Fori(1, GROUPS // U) as it:
                body(it)

            for n in range(len(CHUNKS) + 1):
                if n < len(CHUNKS):
                    a, e = CHUNKS[n][0], CHUNKS[n][-1] + 1
                    act.wait_ge(fin_v, FV_STATS[n])
                    act.activation(fin[:, 0, a:e], mv[:, a:e, 1], ACT.Sqrt, bias=eps[:, 1:2]
                                   ).then_inc(fin_std, 1)
                if n == 0:
                    continue
                act.wait_ge(fin_v, FV_NMR[n - 1])
                for b in CHUNKS[n - 1]:
                    act.activation(acc[:, b, 0:D], acc[:, b, 0:D], ACT.Identity,
                                   scale=fin[:, 1, b:b + 1], bias=fin[:, 2, b:b + 1]
                                   ).then_inc(fin_norm, 1)

        @block.vector
        def _(dve):
            n_cmp = [0]

            def key_step(ins):
                n_cmp[0] += 1
                return ins.then_inc(cmp_done, 1)

            def exchange(lo_out, hi_out, a, b, spare=None):
                if spare is not None:
                    key_step(dve.tensor_copy(spare, b))
                    dve.wait_ge(cmp_done, n_cmp[0])
                    b = spare
                dve.tensor_tensor(lo_out, a, b, ALU.min).then_inc(cmp_done, 1)
                dve.tensor_tensor(hi_out, a, b, ALU.max).then_inc(cmp_done, 1)
                n_cmp[0] += 2

            raw_src, raw_dst = key[0][:].bitcast(I32), key[1][:].bitcast(I32)
            last = slice((CB - 1) * P, TW)
            dve.memset(raw_src[:, last], FIELD).then_inc(pads_set, 1)
            dve.memset(raw_dst[:, last], 0).then_inc(pads_set, 1)
            dve.wait_ge(src_in, 48)
            dve.tensor_scalar(raw_src[0:CP], raw_src[0:CP], SHIFT, None, ALU.logical_shift_left
                              ).then_inc(cmp_done, 1)
            dve.wait_ge(dst_in, 48)
            dve.wait_ge(cmp_done, 1)
            dve.tensor_tensor(raw_src[0:CP], raw_src[0:CP], raw_dst[0:CP], ALU.bitwise_or
                              ).then_inc(cmp_done, 1)
            dve.wait_ge(cmp_done, 2)
            dve.tensor_scalar(raw_src[0:CP], raw_src[0:CP], FLOAT_BIT, None, ALU.bitwise_or
                              ).then_inc(cmp_done, 1)
            n_cmp[0] = 3
            dve.wait_ge(const_in, 16)

            cur = [0]
            low_source = tiles_ps[0:CP]

            def signs(j, source):
                dve.wait_ge(cmp_done, n_cmp[0])
                change = const[0:CP, C_SIGN + j * CB:C_SIGN + (j + 1) * CB]
                key_step(dve.tensor_tensor(
                    key[1 - cur[0]][0:CP, :].rearrange("p (b m) -> p b m", b=CB),
                    source.rearrange("p (b m) -> p b m", b=CB),
                    change.unsqueeze(2).to_broadcast([CP, CB, P]), ALU.mult))
                cur[0] ^= 1
                assert n_cmp[0] == after_sign[j] and cur[0] == buf_sign[j]

            def low_stage(d, source, mirrored=False):
                dve.wait_ge(cmp_done, n_cmp[0])
                a = source.rearrange("p (r t d) -> p r t d", t=2, d=d)
                o = key[1 - cur[0]][0:CP, :].rearrange("p (r t d) -> p r t d", t=2, d=d)
                b, ob = a[:, :, 1, :], o[:, :, 1, :]
                if mirrored:
                    b, ob = b[:, :, ::-1], ob[:, :, ::-1]
                spare = None
                if source is low_source:
                    spare = upper[0:CP, 0:TW // 2].rearrange("p (r d) -> p r d", d=d)
                exchange(o[:, :, 0, :], ob, a[:, :, 0, :], b, spare)
                cur[0] ^= 1

            def high_stage(d, source):
                dve.wait_ge(cmp_done, n_cmp[0])
                pairs, (at, width) = pieces(d)
                o = key[1 - cur[0]][:, 0:NT]
                for first, n, w in pairs:
                    a4 = source[:, first:first + (n - 1) * 2 * d + d + w]
                    o4 = o[:, first:first + (n - 1) * 2 * d + d + w]
                    if n > 1 or w == d:
                        a4 = source[:, first:first + n * 2 * d].rearrange("p (r t d) -> p r t d", t=2, d=d)
                        o4 = o[:, first:first + n * 2 * d].rearrange("p (r t d) -> p r t d", t=2, d=d)
                        spare = upper[:, 0:n * d].rearrange("p (r d) -> p r d", d=d)
                        exchange(o4[:, :, 0], o4[:, :, 1], a4[:, :, 0], a4[:, :, 1],
                                 spare if source is slots_ps else None)
                    else:
                        exchange(o4[:, 0:w], o4[:, d:d + w], a4[:, 0:w], a4[:, d:d + w],
                                 upper[:, first // 2:first // 2 + w] if source is slots_ps else None)
                if width:
                    key_step(dve.tensor_copy(o[:, at:at + width], source[:, at:at + width]))
                cur[0] ^= 1

            signs(0, key[0][0:CP, :])
            for e in range(1, LOW + 1):
                low_stage(1 << (e - 1), key[cur[0]][0:CP, :], mirrored=True)
                for d in (1 << s for s in reversed(range(e - 1))):
                    low_stage(d, key[cur[0]][0:CP, :])
            assert n_cmp[0] == after_low[0]
            for j in range(1, HIGH + 1):
                signs(j, key[cur[0]][0:CP, :])
                if j == 2:
                    dve.wait_ge(std_done, 1)
                    dve.reciprocal(stat[:, 4, :], stat[:, 3, :]).then_inc(rstd_done, 1)
                dve.wait_ge(turned, 2 * j - 1)
                for d in (1 << s for s in reversed(range(j))):
                    high_stage(d, slots_ps if d == 1 << (j - 1) else key[cur[0]][:, 0:NT])
                assert n_cmp[0] == after_high[j] and cur[0] == buf_high[j]
                dve.wait_ge(turned, 2 * j)
                for d in (1 << s for s in reversed(range(LOW))):
                    low_stage(d, low_source if d == P // 2 else key[cur[0]][0:CP, :])
                assert n_cmp[0] == after_low[j]

            dve.wait_ge(cmp_done, n_cmp[0])
            for n in range(2):
                dve.wait_ge(kv_stored[n], 16 * len(CHUNKS[n::2]))
            sorted_i = key[cur[0]][0:CP, :].bitcast(I32)
            for k in (2, 3, 0, 1):
                mask = ((FIELD & ~127), 127)[k % 2] << (SHIFT if k < 2 else 0)
                dve.tensor_scalar(part_i[0:CP, k, :], sorted_i, mask, None, ALU.bitwise_and
                                  ).then_inc(fields_done, 1)
            ends = sorted_i.rearrange("p (b m) -> p b m", b=CB)[:, :, P - 1]
            ends_i = fin[0:CP, 0, 0:CB].bitcast(I32)
            dve.tensor_scalar(ends_i, ends, FIELD << SHIFT, None, ALU.bitwise_and).then_inc(fields_done, 1)
            dve.wait_ge(fields_done, 5)
            dve.tensor_scalar(last_src[0:CP, :], ends_i, 2.0 ** -SHIFT, None, ALU.mult
                              ).then_inc(fields_done, 1)
            dve.wait_ge(fields_done, 6)
            dve.tensor_tensor(below[0:CP], last_src[0:CP].unsqueeze(2).to_broadcast([CP, CB, NB - 1]),
                              const[0:CP, C_EDGE:C_BLOCK].unsqueeze(1).to_broadcast([CP, CB, NB - 1]),
                              ALU.is_lt).then_inc(below_done, 1)
            dve.wait_ge(start_summed, 1)
            dve.tensor_tensor(start[0:NB - 1], start_ps, const[0:NB - 1, C_BLOCK:C_ALL], ALU.add
                              ).then_inc(set_up, 1)
            dve.wait_ge(set_up, 1)
            dve.tensor_scalar(passed[0:NB - 1, :], iota[0:NB - 1, :], start[0:NB - 1, 0:1], None, ALU.is_ge
                              ).then_inc(set_up, 1)
            dve.wait_ge(blocks_summed, 1)
            halves = lambda a: a.rearrange("p (h w) -> p h w", h=2)
            dve.tensor_tensor(halves(tile_of[:]), halves(iota), blk_ps, ALU.subtract).then_inc(set_up, 1)
            dve.tensor_scalar(halves(lsrc[:]), blk_ps, -float(P), None, ALU.mult).then_inc(set_up, 1)
            dve.wait_ge(set_up, 3)
            for b in range(CB):
                dve.tensor_scalar(pick[0:CP, b, :], tile_of[0:CP, :], const[0:CP, C_TILE + b:C_TILE + b + 1],
                                  None, ALU.is_equal).then_inc(set_up, 1)
            dve.wait_ge(visits_picked, 2)
            dve.wait_ge(set_up, 4 + CB)
            dve.tensor_tensor(halves(lsrc[:]), halves(lsrc[:]), vsrc_ps, ALU.add).then_inc(set_up, 1)
            dve.wait_ge(set_up, 5 + CB)

            regs = [dve.alloc_register(f"dve_blk{v}") for v in range(G)]

            def one_hots(i, u):
                dve.tensor_tensor(S[:, u % U, :, :],
                                  iota[:, 0:P].unsqueeze(1).to_broadcast([P, G, P]),
                                  lsrc[:, bass.ds(i * G, G)].unsqueeze(2).to_broadcast([P, G, P]),
                                  ALU.is_equal).then_inc(s_made, 1)

            def load_blocks(i):
                dve.load(regs, blk_i[0:1, bass.ds(i * G, G)])

            def add(i, u, v):
                at = dve.snap(regs[v], min_val=0, max_val=NB - 1)
                block_acc = acc_flat[:, bass.ds(at * RW, RW)]
                if v == 0:
                    dve.wait_ge(summed, i + 1)
                after(dve, added, i * G + v)
                dve.tensor_tensor(block_acc, block_acc, sum_ps(u, v), ALU.add).then_inc(added, 1)

            acc_flat = acc[:].rearrange("p b w -> p (b w)")
            dve.wait_ge(dstf_done, 1)
            for i in range(AHEAD):
                one_hots(i, i)
            dve.wait_ge(acc_zeroed, 1)
            dve.wait_ge(blk_done, 1)

            def body(it, first=False):
                for u in range(U):
                    i = it * U + u
                    k_rows = kv[:, u, :, 0:D]
                    v_rows = kv[:, u, :, D:2 * D]
                    adds = not (first and u == 0)
                    if adds:
                        load_blocks(i - 1)
                    dve.wait_ge(q_spread, i + 1)
                    dve.wait_ge(kv_landed[u], (it + 1) * (G * 16))
                    dve.tensor_tensor(prod[:].rearrange("p (g d) -> p g d", g=G),
                                      q_ps(u).rearrange("p (g d) -> p g d", g=G), k_rows, ALU.mult
                                      ).then_inc(prod_done, 1)
                    if adds:
                        add(i - 1, u + U - 1, 0)
                    dve.wait_ge(prod_done, i + 1)
                    dve.tensor_reduce(att[:], prod[:].rearrange("p (k e) -> p k e", e=HD), AX.X, ALU.add
                                      ).then_inc(red_done, 1)
                    if adds:
                        add(i - 1, u + U - 1, 1)
                    dve.wait_ge(red_done, i + 1)
                    dve.tensor_scalar(attc[:, u % 2, :], att[:], -10.0, 10.0, ALU.max, ALU.min
                                      ).then_inc(clip_done, 1)
                    if adds:
                        add(i - 1, u + U - 1, 2)
                    one_hots(i + AHEAD, u + AHEAD)
                    if adds:
                        add(i - 1, u + U - 1, 3)
                    dve.wait_ge(exp_done, i + 1)
                    w = w_ps(u).rearrange("p (g h) -> p g h", g=G).unsqueeze(3)
                    dve.tensor_tensor(wv[:, u % 2, :, 0:D].rearrange("p g (h e) -> p g h e", e=HD),
                                      v_rows.rearrange("p g (h e) -> p g h e", e=HD),
                                      w.to_broadcast([P, G, N_HEAD, HD]), ALU.mult).then_inc(wv_done, 1)

            body(0, first=True)
            with dve.Fori(1, GROUPS // U) as it:
                body(it)
            load_blocks(GROUPS - 1)
            for v in range(G):
                add(GROUPS - 1, GROUPS - 1, v)

            n_fin = [0]

            def fin_step(ins):
                ins.then_inc(fin_v, 1)
                n_fin[0] += 1

            dve.wait_ge(added, GROUPS * G)
            fin_step(dve.tensor_scalar(rden[:], acc[:, :, D:RW], 1e-8, None, ALU.add))
            dve.wait_ge(fin_v, 1)
            fin_step(dve.reciprocal(rden[:], rden[:]))
            dve.wait_ge(fin_v, 2)

            def stats(n):
                a, e = CHUNKS[n][0], CHUNKS[n][-1] + 1
                y = acc[:, a:e, 0:D].rearrange("p b (h e) -> p b h e", e=HD)
                fin_step(dve.tensor_tensor(y, y, rden[:, a:e, :].unsqueeze(3).to_broadcast(
                    [P, e - a, N_HEAD, HD]), ALU.mult))
                dve.wait_ge(fin_v, n_fin[0])
                fin_step(dve.tensor_tensor(acc[:, a:e, 0:D], acc[:, a:e, 0:D], H[:, a:e, :], ALU.add))
                dve.wait_ge(fin_v, n_fin[0])
                for b in CHUNKS[n]:
                    fin_step(dve.bn_stats(bn[:, b, :], acc[:, b, 0:D]))
                dve.wait_ge(fin_v, n_fin[0])
                for b in CHUNKS[n]:
                    fin_step(dve.bn_aggr(mv[:, b, :], bn[:, b, :]))
                assert n_fin[0] == FV_STATS[n]

            def scales(n):
                a, e = CHUNKS[n][0], CHUNKS[n][-1] + 1
                dve.wait_ge(fin_std, n + 1)
                fin_step(dve.reciprocal(fin[:, 1, a:e], fin[:, 0, a:e]))
                dve.wait_ge(fin_v, n_fin[0])
                fin_step(dve.scalar_tensor_tensor(fin[:, 2, a:e], mv[:, a:e, 0], -1.0, fin[:, 1, a:e],
                                                  ALU.mult, ALU.mult))
                assert n_fin[0] == FV_NMR[n]

            def finish(n):
                a, e = CHUNKS[n][0], CHUNKS[n][-1] + 1
                dve.wait_ge(fin_gam, n + 1)
                if n == 0:
                    dve.wait_ge(xb_done, 1)
                dve.tensor_tensor(X[:, a:e, :], X[:, a:e, :], acc[:, a:e, 0:D], ALU.add
                                  ).then_inc(fin_out, 1)

            for n in range(len(CHUNKS) + 3):
                if n < len(CHUNKS):
                    stats(n)
                if 1 <= n <= len(CHUNKS):
                    scales(n - 1)
                if n >= 3:
                    finish(n - 3)


def kernel(x, src, dst, L0_gnn_Wq, L0_gnn_Wk, L0_gnn_Wv, L0_gnn_gamma, L0_gnn_beta):
    import concourse.bacc as bacc
    from concourse.bass_utils import run_bass_kernel_spmd

    nc = bacc.Bacc("TRN2", target_bir_lowering=False, num_devices=1)
    arrays = {
        "x": x, "src": src, "dst": dst, "Wq": L0_gnn_Wq, "Wk": L0_gnn_Wk, "Wv": L0_gnn_Wv,
        "gamma": L0_gnn_gamma, "beta": L0_gnn_beta, "consts": shape_constants(),
    }
    arrays = {name: np.ascontiguousarray(a) for name, a in arrays.items()}
    aps = {name: nc.dram_tensor(name, a.shape, mybir.dt.from_np(a.dtype), kind="ExternalInput").ap()
           for name, a in arrays.items()}
    out = nc.dram_tensor("out", (N_NODES, D), F32, kind="ExternalOutput").ap()
    gnn_kernel(nc, out=out, **aps)
    result = run_bass_kernel_spmd(nc, [arrays], core_ids=[0])
    return result.results[0]["out"]
```
